# Optimizing a Trainium2 kernel written in Bass

```python
import numpy as np
import jax
import jax.numpy as jnp

def _softmax(x, axis=-1):
    return jax.nn.softmax(x, axis=axis)

def _gelu(x):
    return jax.nn.gelu(x, approximate=True)

def _silu(x):
    return jax.nn.silu(x)

def _sigmoid(x):
    return jax.nn.sigmoid(x)

def _layernorm(x, axis=-1, eps=1e-05):
    m = jnp.mean(x, axis=axis, keepdims=True)
    v = jnp.var(x, axis=axis, keepdims=True)
    return (x - m) / jnp.sqrt(v + eps)

def _scatter_add(tgt, idx, src, axis=0):
    return tgt.at[idx].add(src)

def _segment_sum(src, seg, n):
    return jax.ops.segment_sum(src, seg, n)
kernel_name = 'mk_recurrent_d1_jaxref_r4_32c6dc'

def setup_inputs(seed: int=0):
    np.random.seed(seed)
    _w = jnp.asarray

    def _L0_attn_setup():
        import jax, jax.numpy as jnp
        import numpy as np
        H, D = (8, 128)
        HID = 256
        K = 4
        EPS_QK = 1e-06
        EPS_NORM = 1e-05

        def short_conv(x, w):
            k = w.shape[-1]
            xp = jnp.pad(x, ((0, 0), (k - 1, 0), (0, 0)))
            xc = jnp.transpose(xp, (0, 2, 1))
            y = jax.lax.conv_general_dilated(xc, w, window_strides=(1,), padding='VALID', feature_group_count=w.shape[0])
            return jax.nn.silu(jnp.transpose(y, (0, 2, 1)))

        def _rmsn(t, eps):
            return t * jax.lax.rsqrt(jnp.mean(t * t, axis=-1, keepdims=True) + eps)
        key = jax.random.key(seed)
        ks = jax.random.split(key, 16)
        s = 0.02
        inp = {'x': jax.random.normal(ks[0], (2, 256, HID), dtype=jnp.float32), 'Wq': jax.random.normal(ks[1], (H * D, HID), dtype=jnp.float32) * s, 'Wk': jax.random.normal(ks[2], (H * D, HID), dtype=jnp.float32) * s, 'Wv': jax.random.normal(ks[3], (H * D, HID), dtype=jnp.float32) * s, 'wq_conv': jax.random.normal(ks[4], (H * D, 1, K), dtype=jnp.float32) * 0.3, 'wk_conv': jax.random.normal(ks[5], (H * D, 1, K), dtype=jnp.float32) * 0.3, 'wv_conv': jax.random.normal(ks[6], (H * D, 1, K), dtype=jnp.float32) * 0.3, 'Wfa': jax.random.normal(ks[7], (D, HID), dtype=jnp.float32) * s, 'Wfb': jax.random.normal(ks[8], (H * D, D), dtype=jnp.float32) * s, 'Wb': jax.random.normal(ks[9], (H, HID), dtype=jnp.float32) * s, 'Wga': jax.random.normal(ks[10], (D, HID), dtype=jnp.float32) * s, 'Wgb': jax.random.normal(ks[11], (H * D, D), dtype=jnp.float32) * s, 'A_log': jnp.log(jax.random.uniform(ks[12], (H,), minval=1.0, maxval=16.0, dtype=jnp.float32)), 'dt_bias': jnp.zeros((H, D), dtype=jnp.float32), 'o_norm_w': jnp.ones((D,), dtype=jnp.float32), 'Wo': jax.random.normal(ks[13], (HID, H * D), dtype=jnp.float32) * s}
        return inp
    _L0_attn_in = _L0_attn_setup()

    def _L0_ffn_setup():
        import math
        import jax, jax.numpy as jnp
        import numpy as np
        CAPACITY_FACTOR = 1.25
        key = jax.random.key(seed)
        ks = jax.random.split(key, 5)
        B, S, H, F, E = (4, 1024, 256, 256, 32)
        scale_in = 1.0 / math.sqrt(H)
        scale_mid = 1.0 / math.sqrt(F)
        return {'x': jax.random.normal(ks[0], (B, S, H), dtype=jnp.float32), 'w_router': jax.random.normal(ks[1], (H, E), dtype=jnp.float32) * scale_in, 'w_gate': jax.random.normal(ks[2], (E, H, F), dtype=jnp.float32) * scale_in, 'w_up': jax.random.normal(ks[3], (E, H, F), dtype=jnp.float32) * scale_in, 'w_down': jax.random.normal(ks[4], (E, F, H), dtype=jnp.float32) * scale_mid}
    _L0_ffn_in = _L0_ffn_setup()
    _d = {'L0_attn_x': _L0_attn_in['x'], 'L0_attn_Wq': _L0_attn_in['Wq'], 'L0_attn_Wk': _L0_attn_in['Wk'], 'L0_attn_Wv': _L0_attn_in['Wv'], 'L0_attn_wq_conv': _L0_attn_in['wq_conv'], 'L0_attn_wk_conv': _L0_attn_in['wk_conv'], 'L0_attn_wv_conv': _L0_attn_in['wv_conv'], 'L0_attn_Wfa': _L0_attn_in['Wfa'], 'L0_attn_Wfb': _L0_attn_in['Wfb'], 'L0_attn_Wb': _L0_attn_in['Wb'], 'L0_attn_Wga': _L0_attn_in['Wga'], 'L0_attn_Wgb': _L0_attn_in['Wgb'], 'L0_attn_A_log': _L0_attn_in['A_log'], 'L0_attn_dt_bias': _L0_attn_in['dt_bias'], 'L0_attn_o_norm_w': _L0_attn_in['o_norm_w'], 'L0_attn_Wo': _L0_attn_in['Wo'], 'L0_ffn_w_router': _L0_ffn_in['w_router'], 'L0_ffn_w_gate': _L0_ffn_in['w_gate'], 'L0_ffn_w_up': _L0_ffn_in['w_up'], 'L0_ffn_w_down': _L0_ffn_in['w_down']}
    _x0 = _d['L0_attn_x']
    _d['L0_attn_x'] = jax.random.normal(jax.random.fold_in(jax.random.key(seed), 1), (8, 512, 256), dtype=_x0.dtype)
    del _x0
    return _d

def reference(L0_attn_x, L0_attn_Wq, L0_attn_Wk, L0_attn_Wv, L0_attn_wq_conv, L0_attn_wk_conv, L0_attn_wv_conv, L0_attn_Wfa, L0_attn_Wfb, L0_attn_Wb, L0_attn_Wga, L0_attn_Wgb, L0_attn_A_log, L0_attn_dt_bias, L0_attn_o_norm_w, L0_attn_Wo, L0_ffn_w_router, L0_ffn_w_gate, L0_ffn_w_up, L0_ffn_w_down):

    def _L0_attn_ref(x, Wq, Wk, Wv, wq_conv, wk_conv, wv_conv, Wfa, Wfb, Wb, Wga, Wgb, A_log, dt_bias, o_norm_w, Wo):
        import jax, jax.numpy as jnp
        import numpy as np
        H, D = (8, 128)
        HID = 256
        K = 4
        EPS_QK = 1e-06
        EPS_NORM = 1e-05

        def short_conv(x, w):
            k = w.shape[-1]
            xp = jnp.pad(x, ((0, 0), (k - 1, 0), (0, 0)))
            xc = jnp.transpose(xp, (0, 2, 1))
            y = jax.lax.conv_general_dilated(xc, w, window_strides=(1,), padding='VALID', feature_group_count=w.shape[0])
            return jax.nn.silu(jnp.transpose(y, (0, 2, 1)))

        def _rmsn(t, eps):
            return t * jax.lax.rsqrt(jnp.mean(t * t, axis=-1, keepdims=True) + eps)
        B, T, _ = x.shape
        scale = float(D) ** (-0.5)
        q = short_conv(x @ Wq.T, wq_conv).reshape(B, T, H, D)
        k = short_conv(x @ Wk.T, wk_conv).reshape(B, T, H, D)
        v = short_conv(x @ Wv.T, wv_conv).reshape(B, T, H, D)
        q = scale ** 2 * _rmsn(q, EPS_QK)
        k = scale * _rmsn(k, EPS_QK)
        a_logits = (x @ Wfa.T @ Wfb.T).reshape(B, T, H, D)
        g = -jnp.exp(A_log)[None, None, :, None] * jax.nn.softplus(a_logits + dt_bias)
        beta = jax.nn.sigmoid(x @ Wb.T)

        def step(S, inputs):
            q_t, k_t, v_t, g_t, b_t = inputs
            S = S * jnp.exp(g_t)[..., None]
            kv = jnp.einsum('bhd,bhdv->bhv', k_t, S)
            delta = b_t[..., None] * (v_t - kv)
            S = S + k_t[..., None] * delta[:, :, None, :]
            o = jnp.einsum('bhd,bhdv->bhv', q_t, S)
            return (S, o)
        tb = lambda t: jnp.moveaxis(t, 1, 0)
        S0 = jnp.zeros((B, H, D, D), dtype=x.dtype)
        _, o_t = jax.lax.scan(step, S0, (tb(q), tb(k), tb(v), tb(g), tb(beta)))
        out = jnp.moveaxis(o_t, 0, 1)
        gate = (x @ Wga.T @ Wgb.T).reshape(B, T, H, D)
        out = _rmsn(out, EPS_NORM) * o_norm_w * jax.nn.sigmoid(gate)
        return out.reshape(B, T, H * D) @ Wo.T

    def _L0_ffn_ref(x, w_router, w_gate, w_up, w_down):
        import math
        import jax, jax.numpy as jnp
        import numpy as np
        CAPACITY_FACTOR = 1.25
        B, S, H = x.shape
        E = w_gate.shape[0]
        T = B * S
        C = int(math.ceil(CAPACITY_FACTOR * T / E))
        xt = x.reshape(T, H)
        logits = xt @ w_router
        probs = jax.nn.softmax(logits, axis=-1)
        top1 = jnp.argmax(probs, axis=-1)
        gate = jnp.take_along_axis(probs, top1[:, None], axis=1)[:, 0]
        onehot = jax.nn.one_hot(top1, E, dtype=jnp.int32)
        pos = jnp.cumsum(onehot, axis=0)[jnp.arange(T), top1] - 1
        accepted = pos < C
        slot = jnp.where(accepted, top1 * C + pos, E * C)
        buf = jnp.zeros((E * C + 1, H), dtype=x.dtype).at[slot].set(xt)
        buf = buf[:E * C].reshape(E, C, H)
        g = jnp.einsum('ech,ehf->ecf', buf, w_gate)
        u = jnp.einsum('ech,ehf->ecf', buf, w_up)
        y = jnp.einsum('ecf,efh->ech', jax.nn.silu(g) * u, w_down)
        out_tok = y.reshape(E * C, H)[jnp.clip(slot, 0, E * C - 1)]
        out_tok = jnp.where(accepted[:, None], out_tok * gate[:, None], 0.0)
        return (xt + out_tok).reshape(B, S, H)
    x = L0_attn_x
    xn = _layernorm(x, axis=-1)
    s = _L0_attn_ref(xn, L0_attn_Wq, L0_attn_Wk, L0_attn_Wv, L0_attn_wq_conv, L0_attn_wk_conv, L0_attn_wv_conv, L0_attn_Wfa, L0_attn_Wfb, L0_attn_Wb, L0_attn_Wga, L0_attn_Wgb, L0_attn_A_log, L0_attn_dt_bias, L0_attn_o_norm_w, L0_attn_Wo)
    g = _silu(_L0_ffn_ref(xn, L0_ffn_w_router, L0_ffn_w_gate, L0_ffn_w_up, L0_ffn_w_down))
    x = x + s * g
    return x

_drawn_inputs = setup_inputs


def setup_inputs(seed=0):
    import zlib

    import numpy as np

    out = dict(_drawn_inputs(seed))
    spreads = {'L0_attn_dt_bias': (0.0, 0.8), 'L0_attn_o_norm_w': (1.0, 0.6)}
    factors = {'L0_attn_Wfa': 8.0,
     'L0_attn_Wfb': 8.0,
     'L0_attn_Wb': 8.0,
     'L0_attn_Wga': 8.0,
     'L0_attn_Wgb': 8.0,
     'L0_attn_A_log': 8.0,
     'L0_ffn_w_router': 8.0,
     'L0_ffn_w_gate': 8.0,
     'L0_ffn_w_up': 8.0,
     'L0_ffn_w_down': 8.0}
    for name, (base, spread) in spreads.items():
        noise = np.random.default_rng([zlib.crc32(name.encode()), seed]).standard_normal(out[name].shape)
        drawn = base * np.exp(spread * noise) if base else spread * noise
        out[name] = jnp.asarray(drawn.astype(out[name].dtype))
    for name, factor in factors.items():
        out[name] = (out[name] * factor).astype(out[name].dtype)
    return out
```

```python
import concourse.bass as bass
from concourse import mybir
from contextlib import ExitStack

F32 = mybir.dt.float32
I32 = mybir.dt.int32
U32 = mybir.dt.uint32
ALU = mybir.AluOpType
ACT = mybir.ActivationFunctionType
AX = mybir.AxisListType

B, T, HID = 8, 512, 256
H, D, TAPS = 8, 128, 4
E, F = 32, 256
TOK = B * T
P = 128
KH = HID // P
NC = T // P
NT = TOK // P
SEQS = B * H
CAP = -(-TOK * 5 // (4 * E))
SLOTS = E * CAP
CAPB = CAP - P
HALF = P // 2
Q = 32
NB = P // Q
EPS_QK, EPS_NORM, EPS_LN = 1e-6, 1e-5, 1e-5
Q_EPS = EPS_NORM * float(D) ** 2

W_Q, W_K, W_V, W_F, W_G = 0, KH * D, 2 * KH * D, 3 * KH * D, 3 * KH * D + D
W_CONV = W_G + D
W_DT = W_CONV + 3 * TAPS
W_A = W_DT + 1
W_COLS = W_A + 1
O_COLS = HID + 1
C_ID = 0
C_TRI = C_ID + P
C_ONE = C_TRI + P
C_ID32 = C_ONE + P
C_LOW = C_ID32 + Q
C_REV = C_LOW + 5 * Q
C_TOK = C_REV + E
C_COLS = C_TOK + NT
M_DIAG = 0
M_LEV = P
M_COLS = M_LEV + 5 * HALF


def constants():
    import numpy as np
    p = np.arange(P)[:, None]
    c = np.zeros((P, C_COLS), np.float32)
    j = np.arange(P)[None, :]
    c[:, C_ID:C_ID + P] = p == j
    c[:, C_TRI:C_TRI + P] = p <= j
    c[:, C_ONE:C_ONE + P] = 1.0
    j32 = np.arange(Q)[None, :]
    c[:, C_ID32:C_ID32 + Q] = (p % Q) == j32
    for l in range(5):
        s = 1 << l
        i = p % Q
        c[:, C_LOW + l * Q:C_LOW + (l + 1) * Q] = (i // (2 * s) == j32 // (2 * s)) & (i % (2 * s) >= s) & (j32 % (2 * s) < s)
    c[:, C_REV:C_REV + E] = E - np.arange(E)[None, :]
    c[:, C_TOK:C_TOK + NT] = SLOTS + np.arange(NT)[None, :] * P + p
    m = np.zeros((P, M_COLS), np.int32)
    m[:, M_DIAG:M_DIAG + P] = p == j
    for l in range(5):
        s = 1 << l
        r = np.arange(HALF)[None, :]
        m[:, M_LEV + l * HALF:M_LEV + (l + 1) * HALF] = (p // (2 * s) == r // s) & (p % (2 * s) < s)
    return c, m


class Signal:

    def __init__(self, ctx, nc, name, per):
        self.sem = ctx.enter_context(nc.semaphore(name))
        self.per = per

    def at(self, n, k):
        return n * self.per + k


def stand(eng, passed):
    eng.sem_inc(passed, 1)


def hold(eng, signal, n, k):
    value = signal.at(n, k)
    if isinstance(value, int) and value <= 0:
        return
    eng.wait_ge(signal.sem, value)


def build(nc, x, wpack, wopack, wsmall, wgate, wup, wdown, cst, msk, out, slots, ys):
    ctx = ExitStack()
    with ctx:
        def sb(name, shape, dt=F32):
            return ctx.enter_context(nc.sbuf_tensor(name, shape, dt))

        def bank(name):
            return ctx.enter_context(nc.psum_tensor(name, [P, 512], F32))

        def sig(name, per=1):
            return Signal(ctx, nc, name, per)

        C = sb("C", [P, C_COLS])
        M = sb("M", [P, M_COLS], I32)
        XN = sb("XN", [P, NT, HID])
        XT = sb("XT", [P, KH, TOK])
        ACC = sb("ACC", [P, NT, HID])
        FG = sb("FG", [P, 2, TOK])
        FA, GA = FG[:, 0, :], FG[:, 1, :]
        BETA = sb("BETA", [P, H, NT])
        ident = C[:, C_ID:C_ID + P]
        W = sb("W", [P, W_COLS])
        WO = sb("WO", [P, O_COLS])
        WOS = sb("WOS", [P, HID])
        NEGA = sb("NEGA", [P, 1])
        EXA = sb("EXA", [P, 1])
        Y = sb("Y", [P, 3, T])
        RAW = [sb(f"RAW{p}", [P, 2, T]) for p in range(2)]
        SQ = Y[:, 0:2, :]
        GABS = sb("GABS", [P, T])
        GREL = sb("GREL", [P, T])
        GU = sb("GU", [P, T])
        GL = sb("GL", [P, T])
        DEC = GL
        VR = GU
        KQ = [sb(f"KQ{p}", [P, 2, T]) for p in range(2)]
        MQ = [sb(f"MQ{p}", [P, NC, 2, P]) for p in range(2)]
        K5 = sb("K5", [P, NC, P])
        K6 = sb("K6", [HALF, NC, HALF])
        VS = [sb(f"VS{p}", [P, NC, P]) for p in range(2)]
        KST = sb("KST", [P, NC, P])
        SG = [sb(f"SG{p}", [P, T]) for p in range(2)]
        AT = [sb(f"AT{p}", [P, NC]) for p in range(2)]
        ZK = sb("ZK", [P, 2 * NC])
        ZQ = [sb(f"ZQ{p}", [P, NC]) for p in range(2)]
        CV = [sb(f"CV{p}", [P, NC]) for p in range(2)]
        RC = sb("RC", [P, NC])
        RI = sb("RI", [P, NC])
        EXPO = sb("EXPO", [P, 2 * NC])
        BI = sb("BI", [P, NC, Q])
        BT = sb("BT", [P, NC, Q])
        UU = sb("UU", [P, NC, Q])
        U5 = sb("U5", [P, NC, P])
        BU = sb("BU", [P, NC, HALF])
        B64 = BU[0:HALF, :, :]
        U6 = BU[HALF:P, :, :]
        PI = sb("PI", [P, NC, P])
        PIF = sb("PIF", [P, NC, P])
        ST = [sb(f"ST{p}", [P, P]) for p in range(2)]
        RV = sb("RV", [P, P])
        DL = sb("DL", [P, P])
        FY = sb("FY", [P, NC])
        FR = sb("FR", [P, NC])
        WS = sb("WS", [P, KH, 2 * P + E + H])
        XS = [t[:, 0:2, :].rearrange("p a (b d) -> p (a b) d", d=HID) for t in (KQ[0], RAW[1])]
        XC = [t[:, 0:2, :].rearrange("p a (b d) -> p (a b) d", d=HID) for t in (KQ[1], Y)]
        BST = sb("BST", [P, NC, 6])
        MV = sb("MV", [P, NC, 2])
        VE = sb("VE", [P, NC])
        RS = sb("RS", [P, NC])
        RL = VR[0:E + H, :]
        LG = RAW[0][:, :, :].rearrange("p a (b e) -> p (a b) e", e=E)
        R1 = KQ[0][:, :, :].rearrange("p a (b e) -> p (a b) e", e=E)
        R2 = Y[:, 0:2, :].rearrange("p a (b e) -> p (a b) e", e=E)
        ROW = sb("ROW", [P, 10, NT])
        GATE_ROW = 9
        flat_row = ROW[:, :, :].rearrange("p r t -> p (r t)")
        OSQ, GT = flat_row[:, 0:P], flat_row[:, P:2 * P]
        TOT = WS[:, :, :].rearrange("p k w -> p (k w)")[:, 0:T - NC * 2]
        SCI = sb("SCI", [P, NT], U32)
        GAI = sb("GAI", [P, NT], U32)

        PJ = [bank("PJ0"), bank("PJ1")]
        PL = [bank("PL0"), bank("PL1")]
        PR, PO, PV, PM = bank("PR"), bank("PO"), bank("PV"), bank("PM")

        s_cst, s_ws, s_x = sig("s_cst"), sig("s_ws"), [sig(f"s_x{p}", 16) for p in range(2)]
        s_zero = sig("s_zero")
        s_stats, s_aggr, s_var, s_rstd, s_xc = sig("s_stats"), sig("s_aggr"), sig("s_var"), sig("s_rstd"), sig("s_xc")
        s_xn, s_tr, s_xt0, s_xt1 = sig("s_xn"), sig("s_tr"), sig("s_xt0"), sig("s_xt1")
        s_fa, s_ga, s_rl, s_far, s_gar, s_rls = sig("s_fa"), sig("s_ga"), sig("s_rl"), sig("s_far"), sig("s_gar"), sig("s_rls")
        s_rlt, s_lg, s_bt, s_beta = sig("s_rlt"), sig("s_lg"), sig("s_bt"), sig("s_beta")
        s_rt, s_oh, s_pre, s_ex, s_exd, s_idx = sig("s_rt"), sig("s_oh"), sig("s_pre"), sig("s_ex"), sig("s_exd"), sig("s_idx")
        s_zd, s_sc = sig("s_zd"), sig("s_sc")
        w_ready, wo_ready = sig("w_ready", 16), sig("wo_ready", 16)
        proj = sig("proj", 5)
        fread = sig("fread", 2)
        gu, gl = sig("gu"), sig("gl")
        gr = sig("gr")
        gp = sig("gp", 3)
        nega = sig("nega", 2)
        dec = sig("dec")
        tap = sig("tap", 3)
        conv = sig("conv", 9)
        silu = sig("silu", 2)
        gate = sig("gate")
        sq = sig("sq")
        ssum = sig("ssum", 2)
        zk, zq = sig("zk", 3), sig("zq")
        rinv = sig("rinv")
        vtr = sig("vtr")
        vsc = sig("vsc", NC)
        kq = sig("kq", 8)
        lev = sig("lev", 8)
        mask = sig("mask", 6)
        up5, up6 = sig("up5", 4), sig("up6", 2)
        ks = sig("ks", 7)
        tot = sig("tot", 7)
        ktr, kst = sig("ktr"), sig("kst")
        bnew = sig("bnew", 6)
        btr = sig("btr", 6)
        pif = sig("pif")
        vmm, wmm = sig("vmm", 7), sig("wmm", 7)
        umask = sig("umask", 5)
        u5e, b64, p5, u6, p6 = sig("u5e", 2), sig("b64", 3), sig("p5", 2), sig("u6"), sig("p6")
        wos = sig("wos")
        r1 = sig("r1", NC - 1)
        rv = sig("rv", NC - 1)
        dmm, dl = sig("dmm", NC), sig("dl", NC)
        smm, st = sig("smm", NC - 1), sig("st", NC - 1)
        omm = sig("omm", NC)
        osq, gt = sig("osq", NC), sig("gt", NC)
        oss, fy, fr = sig("oss", NC), sig("fy", NC), sig("fr", NC)
        outm, acc = sig("outm", NC), sig("acc", NC)
        e_w, e_x = [sig(f"e_w{k}", 48) for k in range(4)], [sig(f"e_x{k}", 32) for k in range(4)]
        e_tr, e_xt = sig("e_tr"), sig("e_xt")
        e_gu, e_s, e_h, e_ym, e_y = sig("e_gu", 2), sig("e_s"), sig("e_h"), sig("e_ym"), sig("e_y", 2)
        e_yo = [sig(f"e_yo{p}", 32) for p in range(2)]
        f_g, f_x = [sig(f"f_g{b}") for b in range(B)], [sig(f"f_x{p}", 16) for p in range(2)]
        f_v, f_p, f_s = sig("f_v", 2), sig("f_p"), sig("f_s")
        f_o = [sig(f"f_o{p}", 16) for p in range(2)]

        SUM_N, SUM_AT = 28, (0, 144)

        passed = {e: sig("passed_" + e).sem for e in ("sp", "pe", "dve", "pool")}

        block = ctx.enter_context(nc.Block())

        def head(n):
            return n // B if isinstance(n, int) else n >> 3

        def batch(n):
            return n % B if isinstance(n, int) else n & (B - 1)

        def batches(eng, body):
            body(0, 0, 0)
            body(1, 1, 0)
            with eng.Fori(1, B // 2 - 1) as i:
                body(2 * i, 0, i)
                body(2 * i + 1, 1, i)
            body(B - 2, 0, B // 2 - 1)
            body(B - 1, 1, B // 2 - 1)

        def experts(eng, body):
            for k in range(4):
                body(k, k, 0)
            with eng.Fori(1, E // 4 - 1) as i:
                for k in range(4):
                    body(4 * i + k, k, i)
            for k in range(4):
                body(E - 4 + k, k, E // 4 - 1)

        def steps(eng, step):
            step(0, None, None, 1)
            step(1, 0, None, 0)
            step(2, 1, 0, 1)
            step(3, 2, 1, 0)
            with eng.Fori(2, SEQS // 2) as i:
                n = 2 * i
                step(n, n - 1, n - 2, 1)
                step(n + 1, n, n - 1, 0)
            step(None, SEQS - 1, SEQS - 2, 1)
            step(None, None, SEQS - 1, 0)

        def halves(t, l, side):
            s = 1 << l
            if len(t.shape) == 3:
                return t.rearrange("p a (b u s) -> p a b u s", u=2, s=s)[:, :, :, side, :]
            return t.rearrange("p (b u s) -> p b u s", u=2, s=s)[:, :, side, :]

        tot_at = {}
        at = 0
        for l in range(1, 7):
            tot_at[l] = at
            at += T >> l

        def totals(l, p):
            if l == 0:
                return DEC[:, :]
            if l == 7:
                return AT[p][:, :]
            return TOT[:, tot_at[l]:tot_at[l] + (T >> l)]

        xt_flat = XT[:, :, :].rearrange("p a t -> p (a t)")
        fg_flat = FG[:, :, :].rearrange("p a t -> p (a t)")
        EW = [fg_flat[:, k * 1536:(k + 1) * 1536].rearrange("p (w k f) -> p w k f", w=3, k=KH) for k in range(4)]
        EX = [xt_flat[:, k * 512:(k + 1) * 512].rearrange("p (a d) -> p a d", a=2) for k in range(4)]

        def pair(at, width):
            return [xt_flat[:, at + p * width:at + (p + 1) * width] for p in range(2)]

        EXT = [t.rearrange("p (k c) -> p k c", k=KH) for t in pair(2048, KH * CAP)]
        EH = [t.rearrange("p (k c) -> p k c", k=KH) for t in pair(2048 + 2 * KH * CAP, KH * CAP)]
        ES = [t.rearrange("p (k c) -> p k c", k=KH) for t in pair(2048 + 4 * KH * CAP, KH * CAP)]
        EY = [t.rearrange("p (a d) -> p a d", a=2) for t in pair(2048 + 6 * KH * CAP, 2 * HID)]
        TB, GUB, YB = (PM, PV), ((PJ[0], PJ[1]), (PR, PO)), PL
        YG = FG[:, :, :].rearrange("p a (t d) -> p (a t) d", d=HID)
        FX = [RAW[0], KQ[0]]
        FX = [t[:, :, :].rearrange("p a (b d) -> p (a b) d", d=HID) for t in FX]
        FO = [t[:, 0:2, :].rearrange("p a (b d) -> p (a b) d", d=HID) for t in (KQ[1], Y)]

        def build_experts_sp(sp):
            sp.wait_ge(proj.sem, proj.at(SEQS, 0))
            sp.wait_ge(s_sc.sem, 16 * NT)

            def load(e, k, i):
                hold(sp, e_ym, e, -3)
                stand(sp, passed["sp"])
                for m, w in enumerate((wgate, wup, wdown)):
                    sp.dma_start(EW[k][:, m, :, :], w[bass.ds(e, 1)].rearrange("a (k q) f -> q (a k) f", q=P)
                                 ).then_inc(e_w[k].sem, 16)
                sp.dma_start(EX[k][:, 0, :], slots[bass.ds(e * CAP, P), :]).then_inc(e_x[k].sem, 16)
                sp.dma_start(EX[k][0:CAPB, 1, :], slots[bass.ds(e * CAP + P, CAPB), :]).then_inc(e_x[k].sem, 16)

            experts(sp, load)

            xv = x.rearrange("(t p) d -> p t d", p=P)

            def final(i, p, first):
                b = 2 * i + p
                if not first:
                    sp.wait_ge(f_v.sem, f_v.at(b, 0) - 2)
                    stand(sp, passed["sp"])
                sp.dma_start(FX[p], xv[:, bass.ds(b * NC, NC), :]).then_inc(f_x[p].sem, 16)

            sp.wait_ge(acc.sem, acc.at(SEQS, 0))
            final(0, 0, True)
            final(0, 1, True)
            with sp.Fori(1, B // 2) as i:
                final(i, 0, False)
                final(i, 1, False)

        @block.sync
        def _(sp):
            sp.dma_start(C[:, :], cst).then_inc(s_cst.sem, 16)
            sp.dma_start(M[:, :], msk).then_inc(s_cst.sem, 16)
            sp.dma_start(WS[:, :, :], wsmall).then_inc(s_ws.sem, 16)
            sp.dma_start(W[:, :], wpack[0]).then_inc(w_ready.sem, 16)
            sp.dma_start(WO[:, :], wopack[0]).then_inc(wo_ready.sem, 16)
            xv = x.rearrange("(t p) d -> p t d", p=P)

            def load_x(b, p, i):
                hold(sp, s_xc, b * NC, -NC)
                stand(sp, passed["sp"])
                sp.dma_start(XS[p], xv[:, bass.ds(b * NC, NC), :]).then_inc(s_x[p].sem, 16)

            batches(sp, load_x)
            sp.wait_ge(s_zero.sem, 1)
            n0 = NT * P
            sp.dma_start(slots[0:n0, :].rearrange("(t p) d -> p t d", p=P), ACC[:, :, :]).then_inc(s_zd.sem, 16)
            sp.dma_start(slots[n0:SLOTS, :].rearrange("(t p) d -> p t d", p=P),
                         ACC[:, 0:(SLOTS - n0) // P, :]).then_inc(s_zd.sem, 16)
            with sp.Fori(1, H) as h:
                sp.wait_ge(proj.sem, proj.at(h * B, 0))
                stand(sp, passed["sp"])
                sp.wait_ge(conv.sem, conv.at(h * B, 0))
                stand(sp, passed["sp"])
                sp.wait_ge(dec.sem, dec.at(h * B, 0))
                stand(sp, passed["sp"])
                sp.dma_start(W[:, :], wpack[bass.ds(h, 1)].rearrange("a p w -> p (a w)")).then_inc(w_ready.sem, 16)
                sp.wait_ge(wos.sem, wos.at(h * B, 0))
                stand(sp, passed["sp"])
                sp.dma_start(WO[:, :], wopack[bass.ds(h, 1)].rearrange("a p w -> p (a w)")).then_inc(wo_ready.sem, 16)
            build_experts_sp(sp)

        @block.tensor
        def _(pe):
            mm = nc.tensor.matmul
            pe.wait_ge(s_cst.sem, 32)
            pe.wait_ge(s_ws.sem, 16)

            def transform(b, p, i):
                pe.wait_ge(s_xc.sem, (b + 1) * NC)
                hold(pe, s_xt0, b, 0)
                hold(pe, s_xt1, b, 0)
                for k in range(KH):
                    for c in range(NC):
                        last = nc.tensor.transpose(PJ[k][:, c * P:(c + 1) * P], XC[p][:, c, k * P:(k + 1) * P], ident)
                last.then_inc(s_tr.sem, 1)
                pe.wait_ge(s_xt0.sem, b + 1)
                pe.wait_ge(s_xt1.sem, b + 1)
                rhs = [XT[:, k, bass.ds(b * T, T)] for k in range(KH)]
                hold(pe, s_rls, b, 0)
                stand(pe, passed["pe"])
                for k in range(KH):
                    last = mm(PR[0:E + H, :], WS[:, k, 2 * P:2 * P + E + H], rhs[k], start=k == 0, stop=k == KH - 1)
                last.then_inc(s_rl.sem, 1)
                hold(pe, s_far, b, 0)
                for k in range(KH):
                    last = mm(PL[0][:, :], WS[:, k, 0:P], rhs[k], start=k == 0, stop=k == KH - 1)
                last.then_inc(s_fa.sem, 1)
                hold(pe, s_gar, b, 0)
                for k in range(KH):
                    last = mm(PL[1][:, :], WS[:, k, P:2 * P], rhs[k], start=k == 0, stop=k == KH - 1)
                last.then_inc(s_ga.sem, 1)
                pe.wait_ge(s_rls.sem, b + 1)
                hold(pe, s_lg, b, 0)
                hold(pe, s_bt, b, 0)
                stand(pe, passed["pe"])
                for c in range(NC):
                    last = nc.tensor.transpose(PO[:, c * (E + H):(c + 1) * (E + H)], RL[:, c * P:(c + 1) * P],
                                               ident[0:E + H, 0:E + H])
                last.then_inc(s_rlt.sem, 1)

            batches(pe, transform)
            pe.wait_ge(s_oh.sem, 1)
            oh = R2[:, :, :].rearrange("p t e -> p (t e)")
            for i in range(2):
                mm(PL[i][:, :], C[:, C_TRI:C_TRI + P], oh[:, i * 512:(i + 1) * 512], start=True, stop=True)
            for i in range(2):
                last = mm(PJ[i][:, :], C[:, C_ONE:C_ONE + P], oh[:, i * 512:(i + 1) * 512], start=True, stop=True)
            last.then_inc(s_pre.sem, 1)
            pe.wait_ge(s_idx.sem, 1)
            pe.wait_ge(s_beta.sem, 1)

            def step(na, ni, nr, p):
                a_, i_, r_ = na is not None, ni is not None, nr is not None
                q = 1 - p
                if a_:
                    b = batch(na)

                def project(j):
                    bank_ = PJ[j % 2]
                    if j == 0:
                        pe.wait_ge(w_ready.sem, (head(na) + 1) * 16)
                        hold(pe, gate, na, 0)
                    elif j == 1:
                        hold(pe, vsc, na, 0)
                    elif j == 2:
                        hold(pe, fread, na, 2)
                    elif j == 3:
                        hold(pe, conv, na, 3)
                    else:
                        hold(pe, conv, na, 6)
                    if j in (0, 4):
                        w, src = (W_F, FA) if j == 0 else (W_G, GA)
                        last = mm(bank_[:, :], W[:, w:w + D], src[:, bass.ds(b * T, T)], start=True, stop=True)
                    else:
                        w = (W_K, W_Q, W_V)[j - 1]
                        for k in range(KH):
                            last = mm(bank_[:, :], W[:, w + k * D:w + (k + 1) * D], XT[:, k, bass.ds(b * T, T)],
                                      start=k == 0, stop=k == KH - 1)
                    last.then_inc(proj.sem, 1)

                def squares(a):
                    hold(pe, sq, na, 1)
                    hold(pe, zk, na, -2)
                    if r_:
                        hold(pe, acc, nr, 2)
                    for c in range(NC):
                        last = mm(PO[:, SUM_AT[a] + c * SUM_N:SUM_AT[a] + (c + 1) * SUM_N], SQ[:, a, c * P:(c + 1) * P],
                                  C[:, C_ONE:C_ONE + SUM_N], start=True, stop=True)
                    last.then_inc(ssum.sem, 1)

                def transpose_v():
                    hold(pe, silu, na, 2)
                    hold(pe, conv, na, 9)
                    for c in range(NC):
                        last = nc.tensor.transpose(PJ[1][:, c * P:(c + 1) * P], VR[:, c * P:(c + 1) * P], ident)
                    last.then_inc(vtr.sem, 1)

                def diagonal():
                    hold(pe, silu, ni, 1)
                    hold(pe, up5, ni, 0)
                    for c in range(NC):
                        last = mm(PL[1][:, c * P:(c + 1) * P], RAW[p][:, 0, c * P:(c + 1) * P],
                                  RAW[p][:, 1, c * P:(c + 1) * P], start=True, stop=True)
                    last.then_inc(lev.sem, 1)

                def level(l):
                    hold(pe, kq, ni, l + 1)
                    if l >= 1:
                        hold(pe, ks, ni, l)
                    if l == 0:
                        hold(pe, up6, ni, 0)
                    else:
                        hold(pe, mask, ni, l)
                    for c in range(NC):
                        last = mm(PL[l % 2][:, c * P:(c + 1) * P], RAW[p][:, 0, c * P:(c + 1) * P],
                                  halves(KQ[p][:, :, c * P:(c + 1) * P], l, 1), start=True, stop=True)
                    last.then_inc(lev.sem, 1)

                def inverse_v(l):
                    hold(pe, bnew, ni, l + 1)
                    hold(pe, mask, ni, l + 2)
                    if l == 0:
                        hold(pe, p6, ni, 0)
                    for c in range(NC):
                        last = mm(PV[:, c * Q:(c + 1) * Q], MQ[p][:, c, 0, :], BI[:, c, :], start=True, stop=True)
                    last.then_inc(vmm.sem, 1)

                def inverse_w(l):
                    hold(pe, umask, ni, l + 1)
                    hold(pe, btr, ni, l + 1)
                    for c in range(NC):
                        last = mm(PV[:, P + c * Q:P + (c + 1) * Q], PI[:, c, :], UU[:, c, :], start=True, stop=True)
                    last.then_inc(wmm.sem, 1)

                def neighbours_v():
                    hold(pe, bnew, ni, 6)
                    hold(pe, up5, ni, 4)
                    for c in range(NC):
                        last = mm(PV[:, c * Q:(c + 1) * Q], K5[:, c, :], BI[:, c, :], start=True, stop=True)
                    last.then_inc(vmm.sem, 1)

                def neighbours_w():
                    hold(pe, btr, ni, 6)
                    hold(pe, u5e, ni, 2)
                    for c in range(NC):
                        last = mm(PV[:, P + c * Q:P + (c + 1) * Q], U5[:, c, :], BT[:, c, :], start=True, stop=True)
                    last.then_inc(wmm.sem, 1)

                def halves_v():
                    hold(pe, b64, ni, 3)
                    hold(pe, up6, ni, 2)
                    hold(pe, p5, ni, 2)
                    stand(pe, passed["pe"])
                    for c in range(NC):
                        last = mm(PV[HALF:P, c * HALF:(c + 1) * HALF], K6[:, c, :], B64[:, c, :], start=True, stop=True)
                    last.then_inc(vmm.sem, 1)

                def halves_w():
                    hold(pe, u6, ni, 1)
                    stand(pe, passed["pe"])
                    for c in range(NC):
                        last = mm(PV[0:HALF, 256 + c * HALF:256 + (c + 1) * HALF], U6[:, c, :],
                                  PIF[HALF:P, c, HALF:P], start=True, stop=True)
                    last.then_inc(wmm.sem, 1)

                def transpose_k():
                    hold(pe, ks, ni, 7)
                    hold(pe, kst, ni, 0)
                    if r_:
                        hold(pe, osq, nr, NC)
                        hold(pe, gt, nr, NC)
                    for c in range(NC):
                        last = nc.tensor.transpose(PM[:, c * P:(c + 1) * P], RAW[p][:, 0, c * P:(c + 1) * P], ident)
                    last.then_inc(ktr.sem, 1)

                def carry_in(c):
                    hold(pe, st, nr, c)
                    mm(PR[:, 0:P], KQ[q][:, 0, c * P:(c + 1) * P], ST[c % 2][:, :], start=True, stop=True
                       ).then_inc(r1.sem, 1)

                def delta(c):
                    if c == 0:
                        hold(pe, p6, nr, 1)
                        hold(pe, vsc, nr, NC)
                        rhs = VS[q][:, 0, :]
                    else:
                        hold(pe, rv, nr, c)
                        rhs = RV[:, :]
                    mm(PR[:, P:2 * P], PIF[:, c, :], rhs, start=True, stop=True).then_inc(dmm.sem, 1)

                def state_out(c):
                    hold(pe, dl, nr, c + 1)
                    if c == 0:
                        hold(pe, kst, nr, 1)
                    if c < NC - 1:
                        mm(PR[:, 2 * P:3 * P], KST[:, c, :], DL[:, :], start=True, stop=True).then_inc(smm.sem, 1)
                    hold(pe, osq, nr, c)
                    hold(pe, gt, nr, c)
                    if c > 0:
                        mm(PM[:, 0:P], ST[c % 2][:, :], KQ[q][:, 1, c * P:(c + 1) * P], start=True, stop=False)
                    mm(PM[:, 0:P], DL[:, :], MQ[q][:, c, 1, :], start=c == 0, stop=True).then_inc(omm.sem, 1)

                def project_out(c):
                    hold(pe, osq, nr, c + 1)
                    hold(pe, acc, nr, c)
                    if c == 2 and a_:
                        hold(pe, zk, na, 1)
                    mm(PO[:, 128 + c:129 + c], OSQ[:, :], C[:, C_ONE:C_ONE + 1], start=True, stop=True).then_inc(oss.sem, 1)
                    hold(pe, gt, nr, c + 1)
                    hold(pe, wos, nr, 1)
                    mm(PO[:, 256:512], GT[:, :], WOS[:, :], start=True, stop=True).then_inc(outm.sem, 1)

                if i_: diagonal(); level(0)
                if r_: delta(0)
                if a_: project(0)
                if i_: level(1); inverse_v(0)
                if a_: project(1)
                if i_: inverse_w(0)
                if r_: state_out(0)
                if i_: level(2)
                if r_: carry_in(1)
                if i_: inverse_v(1)
                if a_: project(2)
                if i_: inverse_w(1)
                if r_: delta(1); project_out(0)
                if i_: level(3); inverse_v(2)
                if a_: project(3)
                if r_: state_out(1)
                if i_: inverse_w(2)
                if i_: level(4)
                if i_: inverse_v(3)
                if r_: carry_in(2)
                if a_: project(4)
                if i_: inverse_w(3)
                if r_: delta(2); project_out(1)
                if i_: level(5); inverse_v(4)
                if r_: state_out(2)
                if i_: inverse_w(4)
                if a_: squares(0)
                if i_: level(6)
                if r_: carry_in(3)
                if a_: squares(1)
                if i_: neighbours_v()
                if a_: transpose_v()
                if r_: delta(3)
                if i_: neighbours_w()
                if r_: state_out(3); project_out(2)
                if i_: halves_v(); halves_w(); transpose_k()
                if r_: project_out(3)

            steps(pe, step)

            pe.wait_ge(acc.sem, acc.at(SEQS, 0))

            def slot_transposes(e, k, i):
                pe.wait_ge(e_x[k].sem, e_x[k].at(i, 32))
                hold(pe, e_xt, e, -1)
                bank_ = TB[k % 2]
                for h in range(KH):
                    nc.tensor.transpose(bank_[:, h * CAP:h * CAP + P], EX[k][:, 0, h * P:(h + 1) * P], ident)
                    last = nc.tensor.transpose(bank_[:, h * CAP + P:(h + 1) * CAP], EX[k][0:CAPB, 1, h * P:(h + 1) * P],
                                               ident[0:CAPB, 0:CAPB])
                last.then_inc(e_tr.sem, 1)

            def down(e, k):
                pe.wait_ge(e_h.sem, e_h.at(e, 1))
                hold(pe, e_y, e, -2)
                for (lo, hi), at in (((0, P), 0), ((P, CAP), HID)):
                    for fh in range(KH):
                        last = mm(YB[k % 2][0:hi - lo, at:at + HID], EH[k % 2][:, fh, lo:hi], EW[k][:, 2, fh, :],
                                  start=fh == 0, stop=fh == KH - 1)
                last.then_inc(e_ym.sem, 1)

            def expert(e, k, i):
                if not (isinstance(e, int) and e == E - 1):
                    slot_transposes(e + 1, (k + 1) % 4, i + (k + 1) // 4)
                pe.wait_ge(e_xt.sem, e_xt.at(e, 1))
                pe.wait_ge(e_w[k].sem, e_w[k].at(i, 48))
                hold(pe, e_h, e, -1)
                for w in range(2):
                    for fh in range(KH):
                        for h in range(KH):
                            last = mm(GUB[k % 2][w][:, fh * CAP:(fh + 1) * CAP], EW[k][:, w, h, fh * P:(fh + 1) * P],
                                      EXT[k % 2][:, h, :], start=h == 0, stop=h == KH - 1)
                    last.then_inc(e_gu.sem, 1)
                if not (isinstance(e, int) and e == 0):
                    down(e - 1, (k - 1) % 4)

            slot_transposes(0, 0, 0)
            experts(pe, expert)
            down(E - 1, 3)

        @block.scalar
        def _(act):
            A = nc.scalar.activation

            def copy_x(b, p):
                act.wait_ge(s_xc.sem, (b + 1) * NC)
                A(XN[:, bass.ds(b * NC, NC), :], XC[p], ACT.Copy).then_inc(s_xn.sem, 1)

            def transform(b, p, i):
                act.wait_ge(s_tr.sem, b + 1)
                A(XT[:, 1, bass.ds(b * T, T)], PJ[1][:, :], ACT.Copy).then_inc(s_xt1.sem, 1)
                act.wait_ge(s_rl.sem, b + 1)
                A(RL[:, :], PR[0:E + H, :], ACT.Copy).then_inc(s_rls.sem, 1)
                act.wait_ge(s_fa.sem, b + 1)
                A(FA[:, bass.ds(b * T, T)], PL[0][:, :], ACT.Copy).then_inc(s_far.sem, 1)
                if not (isinstance(b, int) and b == B - 1):
                    copy_x(b + 1, 1 - p)
                act.wait_ge(s_rlt.sem, b + 1)
                A(BETA[:, :, bass.ds(b * NC, NC)],
                  PO[:, 0:NC * (E + H)].rearrange("p (c e) -> p e c", c=NC)[:, E:E + H, :],
                  ACT.Tanh, scale=0.5).then_inc(s_bt.sem, 1)

            copy_x(0, 0)
            batches(act, transform)
            act.wait_ge(s_ex.sem, 1)
            A(LG[:, :, :], LG[:, :, :], ACT.Exp).then_inc(s_exd.sem, 1)

            def step(na, ni, nr, p):
                a_, i_, r_ = na is not None, ni is not None, nr is not None
                q = 1 - p
                dt = W[:, W_DT:W_DT + 1]

                def tap_zero(j):
                    hold(act, proj, na, j + 2)
                    if j == 0:
                        hold(act, ssum, na, 0)
                    A(Y[:, j, :], PJ[(j + 1) % 2][:, :], ACT.Copy,
                      scale=W[:, W_CONV + j * TAPS + TAPS - 1:W_CONV + j * TAPS + TAPS]).then_inc(tap.sem, 1)

                def deltas(c):
                    hold(act, dmm, nr, c + 1)
                    hold(act, omm, nr, c)
                    A(DL[:, :], PR[:, P:2 * P], ACT.Copy).then_inc(dl.sem, 1)

                def out_squares(c):
                    hold(act, omm, nr, c + 1)
                    hold(act, oss, nr, c)
                    A(OSQ, PM[:, 0:P], ACT.Square).then_inc(osq.sem, 1)

                def upper5():
                    hold(act, lev, ni, 7)
                    hold(act, mask, ni, 6)
                    hold(act, vmm, ni, -1)
                    for g in range(2):
                        lo = g * HALF
                        src = PL[1][lo:lo + Q, :].rearrange("p (c k i) -> p c k i", c=NC, k=2)
                        A(K5[lo:lo + Q, :, lo + Q:lo + 2 * Q], src[:, :, 0, g * Q:(g + 1) * Q], ACT.Copy
                          ).then_inc(up5.sem, 1)
                        A(MQ[p][lo:lo + Q, :, 1, lo + Q:lo + 2 * Q], src[:, :, 1, g * Q:(g + 1) * Q], ACT.Copy
                          ).then_inc(up5.sem, 1)

                def upper6():
                    hold(act, lev, ni, 8)
                    src = PL[0][0:HALF, :].rearrange("p (c k i) -> p c k i", c=NC, k=2)
                    A(K6[:, :, :], src[:, :, 0, :], ACT.Copy).then_inc(up6.sem, 1)
                    A(MQ[p][0:HALF, :, 1, HALF:P], src[:, :, 1, :], ACT.Copy).then_inc(up6.sem, 1)

                if a_:
                    act.preload_act_table_set("natural_log_exp_and_others")
                    act.wait_ge(w_ready.sem, (head(na) + 1) * 16)
                    hold(act, dec, na, 0)
                    A(EXA[:, :], W[:, W_A:W_A + 1], ACT.Exp).then_inc(nega.sem, 1)
                if r_: deltas(0)
                if a_:
                    hold(act, proj, na, 1)
                    hold(act, gp, na, 0)
                    A(GABS[:, :], PJ[0][:, :], ACT.Abs, bias=dt).then_inc(fread.sem, 1)
                    A(GREL[:, :], PJ[0][:, :], ACT.Relu, bias=dt).then_inc(fread.sem, 1)
                    hold(act, fread, na, 1)
                    hold(act, vtr, na, 0)
                    A(GU[:, :], GABS[:, :], ACT.Exp, scale=-1.0).then_inc(gu.sem, 1)
                    hold(act, gu, na, 1)
                    hold(act, kq, na, -6)
                    hold(act, ks, na, -6)
                    hold(act, tot, na, -6)
                    A(GL[:, :], GU[:, :], ACT.Ln, bias=1.0).then_inc(gl.sem, 1)
                if r_: out_squares(0)
                if a_: tap_zero(0)
                if a_: tap_zero(1)
                if r_: deltas(1)
                if r_: out_squares(1)
                if a_: tap_zero(2)
                if a_:
                    hold(act, gp, na, 3)
                    hold(act, nega, na, 2)
                    A(DEC[:, :], GREL[:, :], ACT.Exp, scale=NEGA[:, 0:1]).then_inc(dec.sem, 1)
                    hold(act, conv, na, 6)
                    hold(act, ktr, na, -1)
                    A(RAW[q][:, :, :], Y[:, 0:2, :], ACT.Silu).then_inc(silu.sem, 1)
                if r_: deltas(2)
                if r_: out_squares(2)
                if a_:
                    hold(act, silu, na, 1)
                    A(SQ, RAW[q][:, :, :], ACT.Square).then_inc(sq.sem, 1)
                    hold(act, conv, na, 9)
                    A(VR[:, :], Y[:, 2, :], ACT.Silu).then_inc(silu.sem, 1)
                if i_: upper5()
                if i_:
                    upper6()
                if r_: deltas(3)
                if i_:
                    hold(act, btr, ni, 6)
                    hold(act, dmm, ni, 0)
                    A(PIF[:, :, :], PI[:, :, :], ACT.Copy).then_inc(pif.sem, 1)
                if r_: out_squares(3)
                if a_:
                    hold(act, vtr, na, 1)
                    hold(act, rinv, na, 1)
                    hold(act, dmm, na, -NC)
                    for c in range(NC):
                        A(VS[q][:, c, :], PJ[1][:, c * P:(c + 1) * P], ACT.Copy, scale=RI[:, c:c + 1]).then_inc(vsc.sem, 1)
                if a_:
                    hold(act, proj, na, 5)
                    hold(act, gt, na, -NC)
                    A(SG[q][:, :], PJ[0][:, :], ACT.Tanh, scale=0.5).then_inc(gate.sem, 1)
                if i_:
                    hold(act, ktr, ni, 1)
                    hold(act, smm, ni, 0)
                    A(KST[:, :, :].rearrange("p c d -> p (c d)"), PM[:, :], ACT.Copy).then_inc(kst.sem, 1)

            act.wait_ge(s_zero.sem, 1)
            act.wait_ge(s_idx.sem, 1)
            steps(act, step)

            def outputs(e, k, half):
                p = k % 2
                hold(act, e_yo[p], half, 0)
                act.wait_ge(e_ym.sem, e_ym.at(e, 1))
                A(EY[p][:, 0, :], YB[p][:, 0:HID], ACT.Copy).then_inc(e_y.sem, 1)
                A(EY[p][0:CAPB, 1, :], YB[p][0:CAPB, HID:2 * HID], ACT.Copy).then_inc(e_y.sem, 1)
                act.wait_ge(e_y.sem, e_y.at(e, 2))
                act.dma_start(ys[bass.ds(e * CAP, P), :], EY[p][:, 0, :]).then_inc(e_yo[p].sem, 16)
                act.dma_start(ys[bass.ds(e * CAP + P, CAPB), :], EY[p][0:CAPB, 1, :]).then_inc(e_yo[p].sem, 16)

            def expert(e, k, i):
                p = k % 2
                act.wait_ge(e_gu.sem, e_gu.at(e, 1))
                hold(act, e_h, e, -1)
                A(ES[p][:, :, :].rearrange("p k c -> p (k c)"), GUB[p][0][:, 0:KH * CAP], ACT.Silu).then_inc(e_s.sem, 1)
                if not (isinstance(e, int) and e == 0):
                    outputs(e - 1, (k - 1) % 4, 2 * i + (k - 1) // 2)

            experts(act, expert)
            outputs(E - 1, 3, E // 2 - 1)

            ov = out.rearrange("(t p) d -> p t d", p=P)

            def final(i, p, first):
                b = 2 * i + p
                act.wait_ge(f_p.sem, f_p.at(b, 1))
                if not first:
                    act.wait_ge(f_o[p].sem, f_o[p].at(i, 0))
                A(FO[p], XN[:, bass.ds(b * NC, NC), :], ACT.Silu).then_inc(f_s.sem, 1)
                act.wait_ge(f_v.sem, f_v.at(b, 2))
                act.dma_start(ov[:, bass.ds(b * NC, NC), :], FO[p]).then_inc(f_o[p].sem, 16)

            final(0, 0, True)
            final(0, 1, True)
            with act.Fori(1, B // 2) as i:
                final(i, 0, False)
                final(i, 1, False)
            for p in range(2):
                act.wait_ge(f_o[p].sem, f_o[p].at(B // 2, 0))

        @block.vector
        def _(dve):
            V = nc.vector
            V.memset(ACC[:, :, :], 0.0)
            for t in (MQ[0], MQ[1], K5, U5, PI):
                V.memset(t[:], 0.0)
            V.memset(B64, 0.0)
            V.memset(EXPO[:, 0:NC], 0.5)
            V.memset(EXPO[:, NC:2 * NC], -0.5).then_inc(s_zero.sem, 1)
            dve.wait_ge(s_cst.sem, 32)

            def statistics(b, p, i):
                dve.wait_ge(s_x[p].sem, s_x[p].at(i, 16))
                for c in range(NC):
                    V.bn_stats(BST[:, c, :], XS[p][:, c, :]).then_inc(s_stats.sem, 1)
                for c in range(NC):
                    dve.wait_ge(s_stats.sem, b * NC + c + 1)
                    stand(dve, passed["dve"])
                    V.bn_aggr(MV[:, c, :], BST[:, c, :]).then_inc(s_aggr.sem, 1)
                dve.wait_ge(s_aggr.sem, (b + 1) * NC)
                V.tensor_scalar(VE[:, :], MV[:, :, 1], EPS_LN, None, ALU.add).then_inc(s_var.sem, 1)

            def normalise(b, p):
                dve.wait_ge(s_rstd.sem, b + 1)
                hold(dve, s_xn, b, -1)
                hold(dve, s_tr, b, -1)
                for c in range(NC):
                    V.tensor_scalar(XC[p][:, c, :], XS[p][:, c, :], MV[:, c, 0:1], RS[:, c:c + 1], ALU.subtract, ALU.mult
                                    ).then_inc(s_xc.sem, 1)

            def transform(b, p, i):
                more = not (isinstance(b, int) and b == B - 1)
                if more: statistics(b + 1, 1 - p, i + p)
                dve.wait_ge(s_tr.sem, b + 1)
                V.tensor_copy(XT[:, 0, bass.ds(b * T, T)], PJ[0][:, :]).then_inc(s_xt0.sem, 1)
                if more: normalise(b + 1, 1 - p)
                dve.wait_ge(s_ga.sem, b + 1)
                V.tensor_copy(GA[:, bass.ds(b * T, T)], PL[1][:, :]).then_inc(s_gar.sem, 1)
                dve.wait_ge(s_bt.sem, b + 1)
                V.tensor_copy(LG[:, bass.ds(b * NC, NC), :],
                              PO[:, 0:NC * (E + H)].rearrange("p (c e) -> p c e", c=NC)[:, :, 0:E]).then_inc(s_lg.sem, 1)

            statistics(0, 0, 0)
            normalise(0, 0)
            batches(dve, transform)
            rt = [0]

            def link(i):
                rt[0] += 1
                i.then_inc(s_rt.sem, 1)
                dve.wait_ge(s_rt.sem, rt[0])

            dve.wait_ge(s_bt.sem, B)
            V.tensor_scalar(BETA[:, :, :], BETA[:, :, :], 0.5, 0.5, ALU.mult, ALU.add).then_inc(s_beta.sem, 1)
            dve.wait_ge(s_lg.sem, B)
            mx, km, se, pos, ok, slot, scat, gath, tmp, gt_ = (ROW[:, i, :] for i in range(GATE_ROW + 1))

            def over_e(row):
                return row.unsqueeze(2).broadcast_to([P, NT, E])

            link(V.tensor_reduce(mx, LG[:, :, :], AX.X, ALU.max))
            link(V.tensor_tensor(R1[:, :, :], LG[:, :, :], over_e(mx), ALU.is_equal))
            link(V.tensor_tensor(R1[:, :, :], R1[:, :, :],
                                 C[:, C_REV:C_REV + E].unsqueeze(1).broadcast_to([P, NT, E]), ALU.mult))
            link(V.tensor_reduce(km, R1[:, :, :], AX.X, ALU.max))
            V.tensor_tensor(R2[:, :, :], R1[:, :, :], over_e(km), ALU.is_equal).then_inc(s_oh.sem, 1)
            dve.wait_ge(s_oh.sem, 1)
            V.tensor_tensor(LG[:, :, :], LG[:, :, :], over_e(mx), ALU.subtract).then_inc(s_ex.sem, 1)
            dve.wait_ge(s_pre.sem, 1)
            hb = NT // 2
            link(V.memset(R1[:, 0, :], 0.0))
            for t in range(1, NT):
                src = PJ[(t - 1) // hb][:, ((t - 1) % hb) * E:((t - 1) % hb + 1) * E]
                link(V.tensor_tensor(R1[:, t, :], R1[:, t - 1, :], src, ALU.add))
            for i in range(2):
                link(V.tensor_tensor(R1[:, i * hb:(i + 1) * hb, :].rearrange("p t e -> p (t e)"),
                                     R1[:, i * hb:(i + 1) * hb, :].rearrange("p t e -> p (t e)"), PL[i][:, :], ALU.add))
            link(V.tensor_tensor(R1[:, :, :], R1[:, :, :], R2[:, :, :], ALU.mult))
            link(V.tensor_reduce(pos, R1[:, :, :], AX.X, ALU.add))
            link(V.tensor_scalar(ok, pos, float(CAP), None, ALU.is_le))
            link(V.tensor_scalar(tmp, km, -float(CAP), float(SLOTS) - 1.0, ALU.mult, ALU.add))
            link(V.tensor_tensor(slot, tmp, pos, ALU.add))
            link(V.tensor_tensor(scat, slot, C[:, C_TOK:C_TOK + NT], ALU.subtract))
            link(V.tensor_tensor(scat, scat, ok, ALU.mult))
            link(V.tensor_tensor(scat, scat, C[:, C_TOK:C_TOK + NT], ALU.add))
            link(V.tensor_copy(SCI[:, :], scat))
            link(V.tensor_scalar(gath, scat, float(SLOTS - 1), None, ALU.min))
            link(V.tensor_copy(GAI[:, :], gath))
            dve.wait_ge(s_exd.sem, 1)
            link(V.tensor_reduce(se, LG[:, :, :], AX.X, ALU.add))
            link(V.reciprocal(gt_, se))
            V.tensor_tensor(gt_, gt_, ok, ALU.mult).then_inc(s_idx.sem, 1)

            def step(na, ni, nr, p):
                a_, i_, r_ = na is not None, ni is not None, nr is not None
                q = 1 - p

                def convolve(j):
                    src = PJ[(j + 1) % 2]
                    hold(dve, tap, na, j + 1)
                    for i, lag in enumerate((1, 2, 3)):
                        if i:
                            hold(dve, conv, na, 3 * j + i)
                        w = W_CONV + j * TAPS + TAPS - 1 - lag
                        V.scalar_tensor_tensor(Y[:, j, lag:T], src[:, 0:T - lag], W[:, w:w + 1], Y[:, j, lag:T],
                                               ALU.mult, ALU.add).then_inc(conv.sem, 1)

                def transpose_small(n, l, into_bt):
                    hold(dve, bnew, n, l + 2)
                    for g in range(NB):
                        rows = slice(g * Q, (g + 1) * Q)
                        last = V.transpose(PI[rows, :, rows], BI[rows, :, :])
                    if into_bt:
                        last = V.transpose(BT[:, :, :].rearrange("p c q -> p (c q)"),
                                           BI[:, :, :].rearrange("p c q -> p (c q)"))
                    last.then_inc(btr.sem, 1)

                def inverse_first():
                    hold(dve, zk, na, 3)
                    hold(dve, vmm, na, -1)
                    V.tensor_tensor(BI[:, :, :], C[:, C_ID32:C_ID32 + Q].unsqueeze(1).broadcast_to([P, NC, Q]),
                                    CV[q][:, :].unsqueeze(2).broadcast_to([P, NC, Q]), ALU.mult).then_inc(bnew.sem, 1)
                    hold(dve, wmm, na, -1)
                    hold(dve, pif, na, 0)
                    transpose_small(na, -1, False)

                def inverse_u(l):
                    hold(dve, vmm, ni, l + 1)
                    low = C[:, C_LOW + l * Q:C_LOW + (l + 1) * Q].unsqueeze(1).broadcast_to([P, NC, Q])
                    V.tensor_tensor(UU[:, :, :], PV[:, 0:P].rearrange("p (c q) -> p c q", c=NC), low, ALU.mult
                                    ).then_inc(umask.sem, 1)

                def inverse_b(l):
                    hold(dve, wmm, ni, l + 1)
                    V.tensor_tensor(BI[:, :, :], BI[:, :, :], PV[:, P:2 * P].rearrange("p (c q) -> p c q", c=NC),
                                    ALU.subtract).then_inc(bnew.sem, 1)
                    transpose_small(ni, l, l == 4)

                def merge(l):
                    s = 1 << l
                    hold(dve, lev, ni, l + 2)
                    if l:
                        hold(dve, tot, ni, l)
                    hold(dve, kq, ni, l + 1)
                    nb = T // (2 * s)
                    left = totals(l, p).rearrange("p (b u) -> p b u", u=2)[:, :, 0]
                    for a in range(2):
                        right = halves(KQ[p][:, a, :], l, 1)
                        i = V.tensor_tensor(right, right, left.unsqueeze(2).broadcast_to([P, nb, s]), ALU.mult)
                    i.then_inc(kq.sem, 1)

                def keep(l):
                    hold(dve, lev, ni, l + 2)
                    if l < 0:
                        hold(dve, omm, ni, -NC)
                        stand(dve, passed["dve"])
                        V.copy_predicated(MQ[p][:, :, 1, :],
                                          M[:, M_DIAG:M_DIAG + P].unsqueeze(1).broadcast_to([P, NC, P]),
                                          PL[1][:, :].rearrange("p (c i) -> p c i", c=NC)).then_inc(mask.sem, 1)
                        return
                    s = 1 << l
                    nb = HALF // s
                    m = M[:, M_LEV + l * HALF:M_LEV + (l + 1) * HALF].rearrange("p (b s) -> p b s", s=s)
                    hold(dve, mask, ni, l + 1)
                    stand(dve, passed["dve"])
                    V.copy_predicated(halves(MQ[p][:, :, :, :].rearrange("p c k i -> p (c k) i"), l, 1),
                                      m.unsqueeze(1).broadcast_to([P, 2 * NC, nb, s]),
                                      PL[l % 2][:, :].rearrange("p (a b s) -> p a b s", a=2 * NC, s=s)
                                      ).then_inc(mask.sem, 1)

                def next_state(c):
                    hold(dve, smm, nr, c + 1)
                    if c == 0:
                        V.tensor_copy(ST[1][:, :], PR[:, 2 * P:3 * P]).then_inc(st.sem, 1)
                    else:
                        hold(dve, st, nr, c)
                        hold(dve, omm, nr, c)
                        V.scalar_tensor_tensor(ST[(c + 1) % 2][:, :], ST[c % 2][:, :], AT[q][:, c:c + 1],
                                               PR[:, 2 * P:3 * P], ALU.mult, ALU.add).then_inc(st.sem, 1)

                def right_side(c):
                    hold(dve, r1, nr, c)
                    hold(dve, dmm, nr, c)
                    V.tensor_tensor(RV[:, :], VS[q][:, c, :], PR[:, 0:P], ALU.subtract).then_inc(rv.sem, 1)

                def gated(c):
                    hold(dve, omm, nr, c + 1)
                    hold(dve, osq, nr, c + 1)
                    hold(dve, outm, nr, c)
                    V.scalar_tensor_tensor(GT, SG[q][:, c * P:(c + 1) * P], 1.0, PM[:, 0:P], ALU.add, ALU.mult
                                           ).then_inc(gt.sem, 1)

                def out_square(c):
                    hold(dve, outm, nr, c + 1)
                    V.tensor_scalar(FY[:, c:c + 1], PO[:, 128 + c:129 + c], ZQ[q][:, c:c + 1], 1.0 / D,
                                    ALU.add, ALU.mult).then_inc(fy.sem, 1)

                def accumulate(c):
                    hold(dve, outm, nr, c + 1)
                    hold(dve, fr, nr, c + 1)
                    dst = ACC[:, bass.ds(batch(nr) * NC + c, 1), :].rearrange("p a d -> p (a d)")
                    V.scalar_tensor_tensor(dst, PO[:, 256:512], FR[:, c:c + 1], dst, ALU.mult, ALU.add
                                           ).then_inc(acc.sem, 1)

                if a_:
                    hold(dve, nega, na, 1)
                    V.tensor_scalar(NEGA[:, :], EXA[:, :], -1.0, None, ALU.mult).then_inc(nega.sem, 1)
                if i_: merge(0); keep(-1); keep(0)
                if r_:
                    hold(dve, wo_ready, head(nr), 16)
                    hold(dve, outm, nr, 0)
                    V.tensor_scalar(WOS[:, :], WO[:, 0:HID], WO[:, HID:HID + 1], 0.5, ALU.mult, ALU.mult
                                    ).then_inc(wos.sem, 1)
                if i_: merge(1); inverse_u(0); keep(1)
                if a_:
                    hold(dve, gu, na, 1)
                    V.tensor_scalar(GABS[:, :], GU[:, :], 1.0, -1.0, ALU.add, ALU.add).then_inc(gr.sem, 1)
                if i_: inverse_b(0)
                if r_: next_state(0); gated(0)
                if i_: merge(2)
                if r_: right_side(1)
                if i_: inverse_u(1); keep(2)
                if a_: convolve(0)
                if i_: inverse_b(1)
                if i_: merge(3)
                if r_: out_square(0)
                if i_: inverse_u(2); keep(3)
                if a_: convolve(1)
                if i_: inverse_b(2)
                if r_: accumulate(0); next_state(1); gated(1)
                if i_: merge(4)
                if r_: right_side(2)
                if i_: inverse_u(3); keep(4)
                if a_: convolve(2)
                if i_: inverse_b(3)
                if i_: merge(5)
                if r_: out_square(1)
                if i_: inverse_u(4)
                if r_: next_state(2); accumulate(1)
                if i_: inverse_b(4)
                if r_: gated(2)
                if i_: merge(6)
                if r_: right_side(3)
                if i_:
                    hold(dve, vmm, ni, 6)
                    for g in range(2):
                        lo = g * HALF
                        V.tensor_copy(U5[lo + Q:lo + 2 * Q, :, lo:lo + Q],
                                      PV[lo + Q:lo + 2 * Q, 0:P].rearrange("p (c q) -> p c q", c=NC)).then_inc(u5e.sem, 1)
                    for g in range(2):
                        V.tensor_copy(B64[g * Q:(g + 1) * Q, :, g * Q:(g + 1) * Q], BI[g * Q:(g + 1) * Q, :, :]
                                      ).then_inc(b64.sem, 1)
                if a_:
                    hold(dve, ssum, na, 2)
                    hold(dve, rinv, na, 0)
                    sums = PO[:, 0:2 * SUM_AT[1]].rearrange("p (a w) -> p a w", a=2)[:, :, 0:NC * SUM_N]
                    V.tensor_scalar(ZK[:, :].rearrange("p (a c) -> p a c", a=2),
                                    sums.rearrange("p a (c s) -> p a c s", s=SUM_N)[:, :, :, 0],
                                    D * EPS_QK, None, ALU.add).then_inc(zk.sem, 1)
                    hold(dve, zk, na, 1)
                    V.reciprocal(RC[:, :], ZK[:, 0:NC]).then_inc(zk.sem, 1)
                    hold(dve, zk, na, 2)
                    V.tensor_tensor(CV[q][:, :], RC[:, :],
                                    BETA[:, :, :].rearrange("p h t -> p (h t)")[:, bass.ds(na * NC, NC)], ALU.mult
                                    ).then_inc(zk.sem, 1)
                if i_:
                    hold(dve, wmm, ni, 6)
                    hold(dve, pif, ni, 1)
                    for g in range(2):
                        lo = g * HALF
                        V.tensor_scalar(PIF[lo:lo + Q, :, lo + Q:lo + 2 * Q],
                                        PV[lo:lo + Q, P:2 * P].rearrange("p (c q) -> p c q", c=NC), -1.0, None, ALU.mult
                                        ).then_inc(p5.sem, 1)
                    hold(dve, p5, ni, 1)
                    V.transpose(B64[Q:2 * Q, :, 0:Q], PIF[0:Q, :, Q:2 * Q]).then_inc(b64.sem, 1)
                if r_: out_square(2)
                if i_:
                    hold(dve, vmm, ni, 7)
                    V.tensor_copy(U6, PV[HALF:P, 0:256].rearrange("p (c q) -> p c q", c=NC)).then_inc(u6.sem, 1)
                if r_: gated(3); accumulate(2)
                if a_:
                    hold(dve, silu, na, 1)
                    hold(dve, dec, na, 1)
                    hold(dve, omm, na, -NC)
                    V.tensor_tensor(KQ[q][:, :, :], RAW[q][:, :, :],
                                    DEC[:, :].unsqueeze(1).broadcast_to([P, 2, T]), ALU.mult).then_inc(kq.sem, 1)
                if i_:
                    hold(dve, wmm, ni, 7)
                    V.tensor_scalar(PIF[0:HALF, :, HALF:P], PV[0:HALF, 256:512].rearrange("p (c q) -> p c q", c=NC),
                                    -1.0, None, ALU.mult).then_inc(p6.sem, 1)
                if r_: out_square(3)
                if a_:
                    hold(dve, fy, na, -NC)
                    V.tensor_scalar(ZQ[q][:, :], ZK[:, NC:2 * NC], Q_EPS, None, ALU.mult).then_inc(zq.sem, 1)
                    inverse_first()
                if r_: accumulate(3)

            steps(dve, step)

            def slot_tokens(e, k):
                dve.wait_ge(e_tr.sem, e_tr.at(e, 1))
                hold(dve, e_gu, e, -2)
                V.tensor_copy(EXT[k % 2][:, :, :].rearrange("p k c -> p (k c)"), TB[k % 2][:, 0:KH * CAP]
                              ).then_inc(e_xt.sem, 1)

            def expert(e, k, i):
                p = k % 2
                if not (isinstance(e, int) and e == E - 1):
                    slot_tokens(e + 1, (k + 1) % 4)
                dve.wait_ge(e_gu.sem, e_gu.at(e, 2))
                dve.wait_ge(e_s.sem, e_s.at(e, 1))
                hold(dve, e_ym, e, -1)
                V.tensor_tensor(EH[p][:, :, :].rearrange("p k c -> p (k c)"),
                                ES[p][:, :, :].rearrange("p k c -> p (k c)"), GUB[p][1][:, 0:KH * CAP], ALU.mult
                                ).then_inc(e_h.sem, 1)

            slot_tokens(0, 0)
            experts(dve, expert)

            def last(b):
                p = b % 2
                dve.wait_ge(f_s.sem, f_s.at(b, 1))
                V.tensor_tensor(FO[p], FO[p], ACC[:, b * NC:(b + 1) * NC, :], ALU.mult).then_inc(f_v.sem, 1)
                dve.wait_ge(f_x[p].sem, f_x[p].at(b // 2, 16))
                dve.wait_ge(f_v.sem, f_v.at(b, 1))
                V.tensor_tensor(FO[p], FO[p], FX[p], ALU.add).then_inc(f_v.sem, 1)

            for b in range(B):
                dve.wait_ge(f_g[b].sem, 16 * NC)
                for t in range(b * NC, (b + 1) * NC):
                    i = V.scalar_tensor_tensor(XN[:, t, :], YG[:, t, :], gt_[:, t:t + 1], XN[:, t, :], ALU.mult, ALU.add)
                i.then_inc(f_p.sem, 1)
                if b:
                    last(b - 1)
            last(B - 1)

        @block.gpsimd
        def _(pool):
            G = nc.gpsimd
            pool.wait_ge(s_zero.sem, 1)

            def rstd(b, p, i):
                pool.wait_ge(s_var.sem, b + 1)
                hold(pool, s_xc, b * NC, 0)
                G.tensor_tensor(RS[:, :], VE[:, :], EXPO[:, NC:2 * NC], ALU.pow).then_inc(s_rstd.sem, 1)

            batches(pool, rstd)

            def scatter(quarter):
                if quarter == 0:
                    pool.wait_ge(s_idx.sem, 1)
                    pool.wait_ge(s_xn.sem, B)
                    pool.wait_ge(s_zd.sem, 32)
                for t in range(quarter * NT // 4, (quarter + 1) * NT // 4):
                    G.indirect_dma_start(slots[:, :], bass.IndirectOffsetOnAxis(SCI[:, t:t + 1], 0), XN[:, t, :], None
                                         ).then_inc(s_sc.sem, 16)

            def step(na, ni, nr, p):
                a_, i_, r_ = na is not None, ni is not None, nr is not None

                def suffix(l):
                    s = 1 << l
                    hold(pool, lev, ni, l + 2)
                    if l:
                        hold(pool, tot, ni, l)
                        hold(pool, ks, ni, l)
                    if l < 2:
                        hold(pool, kq, ni, 1)
                    pair = totals(l, p).rearrange("p (b u) -> p b u", u=2)
                    left = halves(RAW[p][:, 0, :], l, 0)
                    G.tensor_tensor(left, left, pair[:, :, 1].unsqueeze(2).broadcast_to([P, T // (2 * s), s]), ALU.mult
                                    ).then_inc(ks.sem, 1)
                    if l == 0:
                        hold(pool, kq, ni, 0)
                    if l == 6:
                        hold(pool, st, ni, -(NC - 1))
                    G.tensor_tensor(totals(l + 1, p), pair[:, :, 0], pair[:, :, 1], ALU.mult).then_inc(tot.sem, 1)

                def out_norm(c):
                    hold(pool, fy, nr, c + 1)
                    hold(pool, acc, nr, 0)
                    G.tensor_tensor(FR[:, c:c + 1], FY[:, c:c + 1], EXPO[:, NC:NC + 1], ALU.pow).then_inc(fr.sem, 1)

                if i_: suffix(0)
                if a_:
                    hold(pool, gr, na, 1)
                    G.tensor_tensor(GABS[:, :], GU[:, :], GABS[:, :], ALU.subtract).then_inc(gp.sem, 1)
                if i_: suffix(1)
                if a_:
                    hold(pool, gl, na, 1)
                    G.tensor_tensor(GREL[:, :], GREL[:, :], GL[:, :], ALU.add).then_inc(gp.sem, 1)
                if i_: suffix(2)
                if a_:
                    hold(pool, gp, na, 2)
                    G.tensor_tensor(GREL[:, :], GREL[:, :], GABS[:, :], ALU.add).then_inc(gp.sem, 1)
                if r_: out_norm(0)
                if i_: suffix(3); suffix(4)
                if r_: out_norm(1)
                if i_: suffix(5); suffix(6)
                if a_:
                    hold(pool, zk, na, 1)
                    hold(pool, vsc, na, 0)
                    G.tensor_tensor(RI[:, :], ZK[:, 0:NC], EXPO[:, 0:NC], ALU.pow).then_inc(rinv.sem, 1)
                if r_: out_norm(2); out_norm(3)
                if a_ and isinstance(na, int):
                    scatter(na)

            steps(pool, step)

            for p in range(2):
                pool.wait_ge(e_yo[p].sem, e_yo[p].at(E // 2, 0))
            for t in range(NT):
                G.indirect_dma_start(YG[:, t, :], None, ys[:, :],
                                     bass.IndirectOffsetOnAxis(GAI[:, t:t + 1], 0)).then_inc(f_g[t // NC].sem, 16)


def kernel(L0_attn_x, L0_attn_Wq, L0_attn_Wk, L0_attn_Wv, L0_attn_wq_conv, L0_attn_wk_conv, L0_attn_wv_conv,
           L0_attn_Wfa, L0_attn_Wfb, L0_attn_Wb, L0_attn_Wga, L0_attn_Wgb, L0_attn_A_log, L0_attn_dt_bias,
           L0_attn_o_norm_w, L0_attn_Wo, L0_ffn_w_router, L0_ffn_w_gate, L0_ffn_w_up, L0_ffn_w_down):
    import numpy as np
    import concourse.bacc as bacc
    from concourse.bass_utils import run_bass_kernel_spmd

    def a(v):
        return np.ascontiguousarray(np.asarray(v))

    def by_head(w):
        return a(w).reshape(H, D, KH, P).transpose(0, 3, 2, 1).reshape(H, P, KH * D)

    wpack = np.zeros((H, P, W_COLS), np.float32)
    wpack[:, :, W_Q:W_Q + KH * D] = by_head(L0_attn_Wq)
    wpack[:, :, W_K:W_K + KH * D] = by_head(L0_attn_Wk)
    wpack[:, :, W_V:W_V + KH * D] = by_head(L0_attn_Wv)
    wpack[:, :, W_F:W_F + D] = a(L0_attn_Wfb).reshape(H, D, D).transpose(0, 2, 1)
    wpack[:, :, W_G:W_G + D] = a(L0_attn_Wgb).reshape(H, D, D).transpose(0, 2, 1)
    for j, w in enumerate((L0_attn_wk_conv, L0_attn_wq_conv, L0_attn_wv_conv)):
        wpack[:, :, W_CONV + j * TAPS:W_CONV + (j + 1) * TAPS] = a(w).reshape(H, D, TAPS)
    wpack[:, :, W_DT] = a(L0_attn_dt_bias)
    wpack[:, :, W_A] = a(L0_attn_A_log)[:, None]
    wopack = np.zeros((H, P, O_COLS), np.float32)
    wopack[:, :, 0:HID] = a(L0_attn_Wo).reshape(HID, H, D).transpose(1, 2, 0)
    wopack[:, :, HID] = a(L0_attn_o_norm_w)[None, :]
    wsmall = np.zeros((KH, P, 2 * P + E + H), np.float32)
    wsmall[:, :, 0:P] = a(L0_attn_Wfa).T.reshape(KH, P, P)
    wsmall[:, :, P:2 * P] = a(L0_attn_Wga).T.reshape(KH, P, P)
    wsmall[:, :, 2 * P:2 * P + E] = a(L0_ffn_w_router).reshape(KH, P, E)
    wsmall[:, :, 2 * P + E:] = a(L0_attn_Wb).T.reshape(KH, P, H)
    cst, msk = constants()
    arrays = {
        "x_dram": a(L0_attn_x).reshape(TOK, HID), "wpack_dram": wpack, "wopack_dram": wopack,
        "wsmall_dram": a(wsmall.transpose(1, 0, 2)), "wgate_dram": a(L0_ffn_w_gate), "wup_dram": a(L0_ffn_w_up),
        "wdown_dram": a(L0_ffn_w_down), "cst_dram": cst, "msk_dram": msk,
    }
    nc = bacc.Bacc("TRN2", target_bir_lowering=False, num_devices=1)
    aps = [nc.dram_tensor(n, v.shape, mybir.dt.from_np(v.dtype), kind="ExternalInput").ap() for n, v in arrays.items()]
    out = nc.dram_tensor("out_dram", (TOK, HID), F32, kind="ExternalOutput").ap()
    slots = nc.dram_tensor("slots_dram", (SLOTS + TOK, HID), F32, kind="Internal").ap()
    ys = nc.dram_tensor("expert_out_dram", (SLOTS, HID), F32, kind="Internal").ap()
    build(nc, *aps, out, slots, ys)
    r = run_bass_kernel_spmd(nc, [arrays], core_ids=[0])
    return r.results[0]["out_dram"].reshape(B, T, HID)
```
